# Optimizing a Trainium2 kernel written in Bass

```python
import numpy as np
import jax
import jax.numpy as jnp

def _softmax(x, axis=-1):
    return jax.nn.softmax(x, axis=axis)

def _gelu(x):
    return jax.nn.gelu(x, approximate=True)

def _silu(x):
    return jax.nn.silu(x)

def _sigmoid(x):
    return jax.nn.sigmoid(x)

def _layernorm(x, axis=-1, eps=1e-05):
    m = jnp.mean(x, axis=axis, keepdims=True)
    v = jnp.var(x, axis=axis, keepdims=True)
    return (x - m) / jnp.sqrt(v + eps)

def _scatter_add(tgt, idx, src, axis=0):
    return tgt.at[idx].add(src)

def _segment_sum(src, seg, n):
    return jax.ops.segment_sum(src, seg, n)
kernel_name = 'mk_seq_preln_d1_jaxref_r4_2c2511'

def setup_inputs(seed: int=0):
    np.random.seed(seed)
    _w = jnp.asarray

    def _L0_attn_setup():
        import jax, jax.numpy as jnp
        import numpy as np
        B, N, D = (4, 1024, 256)
        H, DH = (16, 64)
        EPS = 1e-06
        key = jax.random.key(seed)
        ks = jax.random.split(key, 6)
        s = 1.0 / np.sqrt(D)
        return {'x': jax.random.normal(ks[0], (B, N, D), dtype=jnp.float32), 'Wq': jax.random.normal(ks[1], (D, H * DH), dtype=jnp.float32) * s, 'Wk': jax.random.normal(ks[2], (D, H * DH), dtype=jnp.float32) * s, 'Wv': jax.random.normal(ks[3], (D, H * DH), dtype=jnp.float32) * s, 'Wo': jax.random.normal(ks[4], (H * DH, D), dtype=jnp.float32) * s, 'bo': jnp.zeros((D,), dtype=jnp.float32)}
    _L0_attn_in = _L0_attn_setup()

    def _L0_ffn_setup():
        import jax, jax.numpy as jnp
        import numpy as np
        import math
        BETA = 0.9
        THRESHOLD = 1.0
        NUM_STEPS = 5
        ALPHA = 2.0

        @jax.custom_vjp
        def spike_fn(u):
            return (u > 0).astype(u.dtype)

        def _spike_fwd(u):
            return (spike_fn(u), u)

        def _spike_bwd(u, g):
            s = jnp.pi / 2.0 * ALPHA * u
            return (g * (ALPHA / 2.0) / (1.0 + s * s),)
        spike_fn.defvjp(_spike_fwd, _spike_bwd)
        key = jax.random.key(seed)
        k1, k2, k3 = jax.random.split(key, 3)
        n_embd = 256
        x = jax.random.normal(k1, (4, 512, n_embd), dtype=jnp.float32)
        W_fc = jax.random.normal(k2, (4 * n_embd, n_embd), dtype=jnp.float32) / math.sqrt(n_embd)
        W_proj = jax.random.normal(k3, (n_embd, 4 * n_embd), dtype=jnp.float32) / math.sqrt(4 * n_embd)
        return {'x': x, 'W_fc': W_fc, 'W_proj': W_proj}
    _L0_ffn_in = _L0_ffn_setup()
    _d = {'L0_attn_x': _L0_attn_in['x'], 'L0_attn_Wq': _L0_attn_in['Wq'], 'L0_attn_Wk': _L0_attn_in['Wk'], 'L0_attn_Wv': _L0_attn_in['Wv'], 'L0_attn_Wo': _L0_attn_in['Wo'], 'L0_attn_bo': _L0_attn_in['bo'], 'L0_ffn_W_fc': _L0_ffn_in['W_fc'], 'L0_ffn_W_proj': _L0_ffn_in['W_proj']}
    _x0 = _d['L0_attn_x']
    _d['L0_attn_x'] = jax.random.normal(jax.random.fold_in(jax.random.key(seed), 1), (4, 2048, 256), dtype=_x0.dtype)
    del _x0
    return _d

def reference(L0_attn_x, L0_attn_Wq, L0_attn_Wk, L0_attn_Wv, L0_attn_Wo, L0_attn_bo, L0_ffn_W_fc, L0_ffn_W_proj):

    def _L0_attn_ref(x, Wq, Wk, Wv, Wo, bo):
        import jax, jax.numpy as jnp
        import numpy as np
        B, N, D = (4, 1024, 256)
        H, DH = (16, 64)
        EPS = 1e-06

        def split_heads(t):
            b, n, _ = t.shape
            return t.reshape(b, n, H, DH).transpose(0, 2, 1, 3)
        q = split_heads(x @ Wq)
        k = split_heads(x @ Wk)
        v = split_heads(x @ Wv)
        q = jax.nn.elu(q) + 1.0
        k = jax.nn.elu(k) + 1.0
        k_sum = k.sum(axis=2)
        z = jnp.einsum('bhnd,bhd->bhn', q, k_sum)[..., None] + EPS
        kv = jnp.einsum('bhnd,bhne->bhde', k, v)
        out = jnp.einsum('bhnd,bhde->bhne', q, kv) / z
        out = out.transpose(0, 2, 1, 3).reshape(x.shape[0], x.shape[1], H * DH)
        return out @ Wo + bo

    def _L0_ffn_ref(x, W_fc, W_proj):
        import jax, jax.numpy as jnp
        import numpy as np
        import math
        BETA = 0.9
        THRESHOLD = 1.0
        NUM_STEPS = 5
        ALPHA = 2.0

        @jax.custom_vjp
        def spike_fn(u):
            return (u > 0).astype(u.dtype)

        def _spike_fwd(u):
            return (spike_fn(u), u)

        def _spike_bwd(u, g):
            s = jnp.pi / 2.0 * ALPHA * u
            return (g * (ALPHA / 2.0) / (1.0 + s * s),)
        spike_fn.defvjp(_spike_fwd, _spike_bwd)
        h = jnp.square(jax.nn.relu(jnp.einsum('bsd,fd->bsf', x, W_fc)))
        y = jnp.einsum('bsf,df->bsd', h, W_proj)

        def step(mem, _):
            reset = jax.lax.stop_gradient(spike_fn(mem - THRESHOLD))
            mem_new = BETA * mem + y - reset * THRESHOLD
            spk = spike_fn(mem_new - THRESHOLD)
            return (mem_new, spk)
        mem0 = jnp.zeros_like(y)
        _, spks = jax.lax.scan(step, mem0, None, length=NUM_STEPS)
        return jnp.sum(spks, axis=0) / NUM_STEPS
    x = L0_attn_x
    x = x + _L0_attn_ref(_layernorm(x, axis=-1), L0_attn_Wq, L0_attn_Wk, L0_attn_Wv, L0_attn_Wo, L0_attn_bo)
    x = x + _L0_ffn_ref(_layernorm(x, axis=-1), L0_ffn_W_fc, L0_ffn_W_proj)
    return x

_drawn_inputs = setup_inputs


def setup_inputs(seed=0):
    import zlib

    import numpy as np

    out = dict(_drawn_inputs(seed))
    spreads = {'L0_attn_bo': (0.0, 0.1)}
    factors = {'L0_attn_Wq': 3.478}
    for name, (base, spread) in spreads.items():
        noise = np.random.default_rng([zlib.crc32(name.encode()), seed]).standard_normal(out[name].shape)
        drawn = base * np.exp(spread * noise) if base else spread * noise
        out[name] = jnp.asarray(drawn.astype(out[name].dtype))
    for name, factor in factors.items():
        out[name] = (out[name] * factor).astype(out[name].dtype)
    return out
```

```python
from contextlib import ExitStack

import concourse.bass as bass
import numpy as np
from concourse import mybir

ACT = mybir.ActivationFunctionType
ALU = mybir.AluOpType
AX = mybir.AxisListType
F32 = mybir.dt.float32
F16 = mybir.dt.float16

P = 128
HI, LO = 0, 1
PRODUCTS = ((HI, HI), (HI, LO), (LO, HI))

LN_EPS = 1e-5
Z_EPS = 1e-6
QK_SCALE = 16.0
FC_SCALE = 16.0
PROJ_SCALE = 256.0
QN_SCALE = 256.0
M_SCALE = 64.0


def spike_thresholds(beta=0.9, threshold=1.0, steps=5):
    f = np.float32

    def count(y):
        mem, n = f(0), 0
        for _ in range(steps):
            reset = f(1) if mem - f(threshold) > 0 else f(0)
            mem = f(f(f(beta) * mem) + y) - reset * f(threshold)
            n += int(mem - f(threshold) > 0)
        return n

    found = []
    for k in range(1, steps + 1):
        below, above = int(f(0.0).view(np.uint32)), int(f(4.0).view(np.uint32))
        while above - below > 1:
            mid = (below + above) // 2
            if count(np.uint32(mid).view(f)) >= k:
                above = mid
            else:
                below = mid
        found.append(float(np.uint32(below).view(f)))
    return found


def at(chunk, u):
    return chunk + u // 4, u % 4


def wait_past(eng, sem, count):
    if isinstance(count, int) and count <= 0:
        return
    eng.wait_ge(sem, count)


def wait_apart(eng, sem, count, met):
    if not isinstance(count, int):
        count = eng.snap(eng.to_reg(count))
        eng.wait_ge(*met)
    wait_past(eng, sem, count)


def build(nc, x_in, Wq_in, Wk_in, Wv_in, Wo_in, bo_in, Wfc_in, Wproj_in, out):
    B, N, D = x_in.shape
    HD = Wq_in.shape[1]
    F = Wfc_in.shape[0]
    DH = 64
    H = HD // DH
    C2 = D // P
    PAIRS = HD // P
    FB = F // P
    TILES = B * N // P
    CHUNKS = TILES // 4
    BATCH_CHUNKS = CHUNKS // B
    HALF = 512
    assert (D, HD, F, N) == (256, 1024, 1024, 2048)
    THRESHOLDS = spike_thresholds()

    x_rows = x_in.rearrange("b n d -> (b n) d")
    out_rows = out.rearrange("b n d -> (b n) d")
    xT_spill = nc.dram_tensor("xT_spill", [TILES * P, 2 * D], F16).ap()

    ctx = ExitStack()
    with ctx:
        def sb(name, shape, dt):
            return ctx.enter_context(nc.sbuf_tensor(name, shape, dt))

        def sem(name):
            return ctx.enter_context(nc.semaphore(name))

        def sems(name, n):
            return [sem(f"{name}{i}") for i in range(n)]

        wq = sb("wq", [P, 2, C2, HD], F16)
        wfcT = sb("wfcT", [P, 2, FB * C2, P], F16)
        wpT = sb("wpT", [P, 2, C2 * FB, P], F16)
        m_all = sb("m_all", [P, B * 2 * PAIRS * D], F16)
        stage = m_all[:, :].bitcast(F32).rearrange("p (w n) -> p w n", w=4)
        ks_all = sb("ks_all", [P, B * HD], F32)
        wnat = ks_all[:, :].bitcast(F16).rearrange("p (w h n) -> p w h n", w=2, h=2)
        qT = sb("qT", [P, 4, 2 * PAIRS, P], F16)
        kacc = qT[:, :, :, :].rearrange("p a b c -> p (a b c)").bitcast(F32).rearrange("p (b n) -> p b n", b=B)
        h = sb("h", [P, 2, 2, FB, HALF], F16)
        gT = h[:, :, :, :, :].rearrange("p a b c d -> p (a b c d)").bitcast(F32).rearrange(
            "p (b c n) -> p b c n", b=B, c=C2)
        x2 = sb("x2", [P, 16 * D], F32)
        wv = x2[:, 0:C2 * HD].rearrange("p (c n) -> p c n", c=C2)
        wo = x2[:, C2 * HD:C2 * HD + PAIRS * D].rearrange("p (j n) -> p j n", j=PAIRS)
        xn2T = sb("xn2T", [P, 2, 2 * C2, HALF], F16)
        wk = xn2T[:, :, :, :].rearrange("p a b c -> p (a b c)").rearrange("p (h c n) -> p h c n", h=2, c=C2)
        h_f = sb("h_f", [P, 4, HALF], F32)
        kvT = h_f[:, :, :].rearrange("p a b -> p (a b)").rearrange("p (r j n) -> p r j n", r=2, j=PAIRS)
        h_r = sb("h_r", [P, 2, HALF], F32)
        feat = sb("feat", [P, 2, HD], F32)
        feat16 = sb("feat16", [P, 2, 2, HD], F16)
        xnat = sb("xnat", [P, 4, 2, D], F16)
        xT = sb("xT", [P, 4, 2 * C2, P], F16)
        x_t = sb("x_t", [P, 4, D], F32)
        xn = sb("xn", [P, 2, D], F32)
        out_t = sb("out_t", [P, 4, D], F32)
        spikes = sb("spikes", [P, D], F32)
        bo_all = sb("bo_all", [P, D], F32)
        ones = sb("ones", [P, P], F32)
        ln16 = sb("ln16", [P, 1], F32)
        eps = sb("eps", [P, 1], F32)
        bn6 = sb("bn6", [P, 4, 6], F32)
        mv = sb("mv", [P, 4, 2], F32)
        logv = sb("logv", [P, 4], F32)
        seed = sb("seed", [P, 4], F32)
        newt = sb("newt", [P, 4, 3], F32)
        zsum = sb("zsum", [P, 2, H], F32)
        zeps = sb("zeps", [P, 2, H], F32)
        rz = sb("rz", [P, 2, H], F32)
        rk = sb("rk", [P, PAIRS], F32)
        rks = sb("rks", [P, B, PAIRS], F32)

        proj = ctx.enter_context(nc.psum_tensor("proj", [P, 2, HD], F32))
        acc = ctx.enter_context(nc.psum_tensor("acc", [P, 4, HALF], F32))

        consts_ready = sem("consts_ready")
        kvT_zeroed = sem("kvT_zeroed")
        w_loaded = {n: sem(f"w_loaded_{n}") for n in ("k", "fc", "proj", "q", "v", "o", "bo")}
        w_hi = sem("w_hi")
        w_split = sem("w_split")
        w_turned = sems("w_turned", 4)
        xa_loaded = sems("xa_loaded", 4)
        xnT_ready = sems("xnT_ready", 4)
        xnT_spilled = sems("xnT_spilled", 4)
        k_proj, k_neg, k_exp, k_elu = sem("k_proj"), sem("k_neg"), sem("k_exp"), sem("k_elu")
        k_hi, k_lo = sem("k_hi"), sem("k_lo")
        k_added = sem("k_added")
        g_done = sem("g_done")
        g_copied = sem("g_copied")
        chain_full, chain_free = sem("chain_full"), sem("chain_free")
        ks_copied, rk_ready, rks_ready = sem("ks_copied"), sem("rk_ready"), sem("rks_ready")
        kvT_ready = sem("kvT_ready")
        m_hi = sem("m_hi")
        xT_loaded = sems("xT_loaded", 4)
        xb_loaded = sems("xb_loaded", 4)
        q_proj, q_neg, q_exp, q_elu = sem("q_proj"), sem("q_neg"), sem("q_exp"), sem("q_elu")
        q_ks, q_z, q_zeps, q_rz = sem("q_ks"), sem("q_z"), sem("q_zeps"), sem("q_rz")
        q_norm, q_hi, q_lo = sem("q_norm"), sem("q_hi"), sem("q_lo")
        qT_ready = sems("qT_ready", 4)
        o_done, x_biased, x2_done = sem("o_done"), sem("x_biased"), sem("x2_done")
        xn2T_ready = sems("xn2T_ready", 4)
        f1_done, h_relu, h_sq, h_hi, h_lo = (sem(n) for n in ("f1_done", "h_relu", "h_sq", "h_hi", "h_lo"))
        f2_done = sem("f2_done")
        spike_steps = sem("spike_steps")
        out_ready = sem("out_ready")
        out_stored = sems("out_stored", 4)

        class LayerNorm:

            def __init__(self, name):
                self.bn, self.stats = sem(name + "_bn"), sem(name + "_stats")
                self.log, self.seed = sem(name + "_log"), sem(name + "_seed")
                self.newton = sem(name + "_newton")
                self.norm, self.hi, self.lo = sem(name + "_norm"), sem(name + "_hi"), sem(name + "_lo")

        ln1, ln2 = LayerNorm("ln1"), LayerNorm("ln2")

        block = ctx.enter_context(nc.Block())

        def live(c, u=0):
            return not isinstance(c, int) or 0 <= 4 * c + u < TILES

        def rows(c, u):
            return bass.ds((4 * c + u) * P, P)

        def x2_at(c, u):
            return x2[:, bass.ds((c % 4) * (4 * D) + u * D, D)]

        def m_at(c, part, j):
            return m_all[:, bass.ds((c // BATCH_CHUNKS) * (2 * PAIRS * D) + (part * PAIRS + j) * D, D)]

        def ks_at(c):
            return ks_all[:, bass.ds((c // BATCH_CHUNKS) * HD, HD)]

        def quads(eng, body):
            for b in range(B):
                first = b * BATCH_CHUNKS
                body(first, b)
                end = first + BATCH_CHUNKS - (b == B - 1)
                with eng.Fori(first + 1, end) as c:
                    body(c, None)
            body(CHUNKS - 1, None)

        def chunks(eng, body):
            for s in range(4):
                body(s, s % 2)
            with eng.Fori(0, (CHUNKS - 4) // 2) as i:
                body(2 * i + 4, 0)
                body(2 * i + 5, 1)
            for s in range(CHUNKS, CHUNKS + 3):
                body(s, s % 2)

        def chain_jobs(b):
            return ([("ksum column", b, 0)] + [("kv", b, i) for i in range(2)],
                    [("m", b, i) for i in range(PAIRS // 2)])

        (kv0, m0), (kv1, m1), (kv2, m2), (kv3, m3) = (chain_jobs(b) for b in range(B))
        CHAIN = [[("ksum", b, i) for b in range(B) for i in range(2)], kv0 + kv1, m0 + kv2 + m1, kv3 + m2 + m3]
        JOBS = [j for part in CHAIN for j in part]

        @block.sync
        def _(sp):
            met = (xa_loaded[0], 16)

            def load_x(c, u, loaded):
                sp.dma_start(x_t[:, u, :], x_rows[rows(c, u), :]).then_inc(loaded[u], 16)

            def load_weight(w, dst, src):
                sp.dma_start(dst, src).then_inc(w_loaded[w], 16)

            def turn_xn(c, u):
                wait_apart(sp, ln1.lo, 4 * c + u + 1, met)
                wait_apart(sp, k_proj, 4 * c + u - 3, met)
                wait_apart(sp, xnT_spilled[u], 16 * c, met)
                sp.dma_start_transpose(xT[:, u, :, :], xnat[:, u, :, :].rearrange("p h d -> p (h d)")
                                       ).then_inc(xnT_ready[u], 16)

            def spill_xn(c, u):
                wait_apart(sp, xnT_ready[u], 16 * (c + 1), met)
                sp.dma_start(xT_spill[rows(c, u), :], xT[:, u, :, :].rearrange("p a b -> p (a b)")
                             ).then_inc(xnT_spilled[u], 16)

            def load_x_a(c, u):
                wait_apart(sp, ln1.norm, 4 * c + u - 3, met)
                load_x(c, u, xa_loaded)

            for u in range(4):
                load_x(0, u, xa_loaded)
            load_weight("k", stage[:, 0, :].rearrange("p (c n) -> p c n", c=C2), Wk_in.rearrange("(c p) n -> p c n", p=P))
            sp.wait_ge(*met)
            turn_xn(0, 0)
            for u in range(4, 7):
                load_x_a(*at(0, u))
            turn_xn(0, 1)
            spill_xn(0, 0)

            def a_chunk(c):
                for u in range(4):
                    if live(*at(c, u + 2)):
                        turn_xn(*at(c, u + 2))
                    if live(*at(c, u + 7)):
                        load_x_a(*at(c, u + 7))
                    if live(*at(c, u + 1)):
                        spill_xn(*at(c, u + 1))

            def turn_weight(w, part, dst):
                sp.wait_ge(w_split, 8 + 4 * w)
                sp.dma_start_transpose(dst[:, part, :, :], wnat[:, w, part, :]).then_inc(w_turned[2 * w + part], 16)

            a_chunk(0)
            load_weight("fc", stage[:, 1, :].rearrange("p (f d) -> p f d", f=FB), Wfc_in.rearrange("(f p) d -> p f d", p=P))
            load_weight("v", wv, Wv_in.rearrange("(c p) n -> p c n", p=P))
            with sp.Fori(1, 5) as c:
                a_chunk(c)
            load_weight("proj", stage[:, 2, :].rearrange("p (c f) -> p c f", c=C2), Wproj_in.rearrange("(c p) f -> p c f", p=P))
            load_weight("o", wo, Wo_in.rearrange("(j p) d -> p j d", p=P))
            for part in (HI, LO):
                turn_weight(0, part, wfcT)
            with sp.Fori(5, 9) as c:
                a_chunk(c)
            load_weight("q", stage[:, 3, :].rearrange("p (c n) -> p c n", c=C2), Wq_in.rearrange("(c p) n -> p c n", p=P))
            load_weight("bo", bo_all[:, :], bo_in.partition_broadcast(P))
            for part in (HI, LO):
                turn_weight(1, part, wpT)
            with sp.Fori(9, 14) as c:
                a_chunk(c)
            a_chunk(14)
            a_chunk(15)

            def load_xT(c, u):
                wait_apart(sp, q_proj, 4 * c + u - 3, met)
                sp.dma_start(xT[:, u, :, :].rearrange("p a b -> p (a b)"), xT_spill[rows(c, u), :]
                             ).then_inc(xT_loaded[u], 16)

            def load_x_b(c, u):
                wait_apart(sp, x2_done, 4 * c + u - 3, met)
                load_x(c, u, xb_loaded)

            def turn_q(c, u):
                wait_apart(sp, q_lo, 4 * c + u + 1, met)
                wait_apart(sp, o_done, 4 * c + u - 3, met)
                sp.dma_start_transpose(qT[:, u, :, :], feat16[:, u % 2, :, :].rearrange("p h n -> p (h n)")
                                       ).then_inc(qT_ready[u], 16)

            def turn_xn2(c, u, par):
                wait_apart(sp, ln2.lo, 4 * c + u + 1, met)
                wait_apart(sp, f1_done, FB * (c - 1), met)
                sp.dma_start_transpose(xn2T[:, par, :, u * P:(u + 1) * P], xnat[:, u, :, :].rearrange("p h d -> p (h d)")
                                       ).then_inc(xn2T_ready[u], 16)

            def store_out(c, u):
                wait_apart(sp, out_ready, 4 * c + u + 1, met)
                sp.dma_start(out_rows[rows(c, u), :], out_t[:, u, :]).then_inc(out_stored[u], 16)

            for u in range(4):
                sp.wait_ge(xnT_spilled[u], 16 * CHUNKS)
            sp.wait_ge(k_proj, TILES)
            for u in range(3):
                load_xT(0, u)
            sp.wait_ge(ln1.norm, TILES)

            def b_chunk(s, par):
                for t in range(4):
                    if live(*at(s, t + 3)):
                        load_xT(*at(s, t + 3))
                    if live(s, t):
                        load_x_b(s, t)
                    if live(*at(s, t - 13)):
                        store_out(*at(s, t - 13))
                    if live(*at(s, t - 5)):
                        c, u = at(s, t - 5)
                        turn_xn2(c, u, (par + t // 4 + (t - 5) // 4) % 2)
                    if live(*at(s, t - 1)):
                        if isinstance(s, int) and 4 * s + t - 1 == 0:
                            sp.wait_ge(chain_full, len(CHAIN[0]))
                        turn_q(*at(s, t - 1))

            for s in range(4):
                b_chunk(s, s % 2)
            with sp.Fori(0, (CHUNKS - 6) // 2) as i:
                b_chunk(2 * i + 4, 0)
                b_chunk(2 * i + 5, 1)
            for s in range(CHUNKS - 2, CHUNKS + 4):
                b_chunk(s, s % 2)
            for u in range(4):
                sp.wait_ge(out_stored[u], 16 * CHUNKS)

        @block.tensor
        def _(pe):
            def project(slot, u, w):
                for half in range(2):
                    n = 0
                    for c2 in range(C2):
                        for left, right in PRODUCTS:
                            n += 1
                            mm = pe.matmul(proj[:, slot, half * HALF:(half + 1) * HALF], xT[:, u, left * C2 + c2, :],
                                           w[:, right, c2, half * HALF:(half + 1) * HALF],
                                           start=(n == 1), stop=(n == C2 * len(PRODUCTS)))
                return mm

            def k_tile(c, u):
                pe.wait_ge(xnT_ready[u], 16 * (c + 1))
                wait_past(pe, k_elu, 4 * c + u - 1)
                project(u % 2, u, wk).then_inc(k_proj, 1)

            def g_tile(c, u, first):
                pe.wait_ge(k_lo, 4 * c + u + 1)
                for c2 in range(C2):
                    for half in range(2):
                        for n, (left, right) in enumerate(PRODUCTS):
                            mm = pe.matmul(acc[:, c2 * 2 + half, :], xnat[:, u, left, c2 * P:(c2 + 1) * P],
                                           feat16[:, u % 2, right, half * HALF:(half + 1) * HALF],
                                           start=(first and n == 0), stop=True, skip_group_check=True)
                mm.then_inc(g_done, 1)

            def a_chunk(c, b):
                for u in range(4):
                    first = b is not None and u == 0
                    if first:
                        if live(*at(c, u + 2)):
                            k_tile(*at(c, u + 2))
                        wait_past(pe, g_copied, 4 * b)
                    g_tile(c, u, first)
                    if not first and live(*at(c, u + 2)):
                        k_tile(*at(c, u + 2))

            pe.wait_ge(w_split, 4)
            k_tile(0, 0)
            k_tile(0, 1)
            quads(pe, a_chunk)

            def chain_job(n):
                kind, b, i = JOBS[n]
                bank = acc[:, n % 4, :]
                wait_past(pe, chain_free, n - 3)
                if kind == "ksum":
                    mm = pe.matmul(bank, ones[:, :], kacc[:, b, i * HALF:(i + 1) * HALF], start=True, stop=True)
                elif kind == "ksum column":
                    pe.wait_ge(ks_copied, 2 * (b + 1))
                    for j in range(PAIRS):
                        o = b * HD + j * P
                        mm = pe.transpose(bank[:, j:j + 1], ks_all[0:1, o:o + P], ones[0:1, 0:1])
                elif kind == "kv":
                    for j in range(4 * i, 4 * i + 4):
                        for c2 in range(C2):
                            mm = pe.matmul(bank[:, (j % 4) * P:(j % 4 + 1) * P], wv[:, c2, j * P:(j + 1) * P],
                                           gT[:, b, c2, j * P:(j + 1) * P], start=(c2 == 0), stop=(c2 == C2 - 1))
                else:
                    pe.wait_ge(kvT_ready, 2 * (b + 1))
                    for j in (2 * i, 2 * i + 1):
                        mm = pe.matmul(bank[:, (j % 2) * D:(j % 2 + 1) * D], kvT[:, b % 2, j, :], wo[:, j, :],
                                       start=True, stop=True)
                mm.then_inc(chain_full, 1)

            def q_tile(c, u):
                pe.wait_ge(xT_loaded[u], 16 * (c + 1))
                wait_past(pe, q_elu, 4 * c + u - 1)
                project(u % 2, u, wq).then_inc(q_proj, 1)

            def o_tile(c, u):
                pe.wait_ge(qT_ready[u], 16 * (c + 1))
                wait_past(pe, x2_done, 4 * c + u)
                n = 0
                for j in range(PAIRS):
                    for left, right in PRODUCTS:
                        n += 1
                        mm = pe.matmul(acc[:, 0, 0:D], qT[:, u, left * PAIRS + j, :], m_at(c, right, j),
                                       start=(n == 1), stop=(n == PAIRS * len(PRODUCTS)))
                mm.then_inc(o_done, 1)

            def f1_block(c, par, f):
                if f == 0:
                    for u in range(4):
                        pe.wait_ge(xn2T_ready[u], 16 * (c + 1))
                wait_past(pe, h_sq, FB * c + f - 1)
                n = 0
                for c2 in range(C2):
                    for left, right in PRODUCTS:
                        n += 1
                        mm = pe.matmul(acc[:, 2 + f % 2, :], wfcT[:, left, f * C2 + c2, :], xn2T[:, par, right * C2 + c2, :],
                                       start=(n == 1), stop=(n == C2 * len(PRODUCTS)))
                mm.then_inc(f1_done, 1)

            def f2_tile(c, par, u):
                if u == 0:
                    pe.wait_ge(h_lo, FB * (c + 1))
                wait_past(pe, spike_steps, 5 * (4 * c + u))
                n = 0
                for f in range(FB):
                    for left, right in PRODUCTS:
                        n += 1
                        mm = pe.matmul(acc[:, 1, 0:D], h[:, par, left, f, u * P:(u + 1) * P], wpT[:, right, f::FB, :],
                                       start=(n == 1), stop=(n == FB * len(PRODUCTS)))
                mm.then_inc(f2_done, 1)

            def b_chunk(s, par):
                for t in range(4):
                    if live(s, t):
                        q_tile(s, t)
                    if live(s - 3):
                        f2_tile(s - 3, (par + 1) % 2, t)
                    if live(*at(s, t - 3)):
                        if isinstance(s, int) and s == 0:
                            pe.wait_ge(chain_free, len(JOBS))
                            pe.wait_ge(m_hi, B * PAIRS)
                        o_tile(*at(s, t - 3))
                    if live(s - 2):
                        f1_block(s - 2, par, 2 * t)
                        f1_block(s - 2, par, 2 * t + 1)
                    if isinstance(s, int) and s == 0:
                        pass

            done = 0
            pe.wait_ge(w_split, 16)
            pe.wait_ge(k_elu, TILES)
            q_tile(0, 0)
            q_tile(0, 1)
            pe.wait_ge(k_added, TILES + 1)
            pe.wait_ge(g_copied, 4 * B)
            pe.wait_ge(consts_ready, 3)
            pe.wait_ge(w_loaded["v"], 16)
            pe.wait_ge(w_loaded["o"], 16)
            for part, tile_after in ((0, None), (1, 2), (2, 3), (3, None)):
                for _job in CHAIN[part]:
                    chain_job(done)
                    done += 1
                if tile_after is not None:
                    q_tile(0, tile_after)
            pe.wait_ge(chain_free, len(JOBS))
            for i in range(4):
                pe.wait_ge(w_turned[i], 16)
            o_tile(0, 0)
            for s in range(1, 4):
                b_chunk(s, s % 2)
            with pe.Fori(0, (CHUNKS - 4) // 2) as i:
                b_chunk(2 * i + 4, 0)
                b_chunk(2 * i + 5, 1)
            for s in range(CHUNKS, CHUNKS + 3):
                b_chunk(s, s % 2)

        @block.scalar
        def _(act):
            def seed_rstd(ln, c, u):
                act.wait_ge(ln.stats, 4 * c + u + 1)
                act.activation(logv[:, u:u + 1], mv[:, u, 1:2], ACT.Ln, bias=eps[:, :]).then_inc(ln.log, 1)
                act.wait_ge(ln.log, 4 * c + u + 1)
                act.activation(seed[:, u:u + 1], logv[:, u:u + 1], ACT.Exp, scale=-0.5).then_inc(ln.seed, 1)

            def xn_hi(ln, c, u):
                act.wait_ge(ln.norm, 4 * c + u + 1)
                act.activation(xnat[:, u, HI, :], xn[:, u % 2, :], ACT.Copy).then_inc(ln.hi, 1)

            def exp_part(slot, u, neg, exp, count):
                act.activation(feat[:, u % 2, :], proj[:, slot, :], ACT.Relu, scale=-1.0 / QK_SCALE).then_inc(neg, 1)
                act.wait_ge(neg, count)
                act.activation(feat[:, u % 2, :], feat[:, u % 2, :], ACT.Exp, bias=ln16[:, :], scale=-1.0).then_inc(exp, 1)

            def k_exp_tile(c, u):
                act.wait_ge(k_proj, 4 * c + u + 1)
                wait_past(act, k_lo, 4 * c + u - 1)
                wait_past(act, k_added, 4 * c + u if live(c, u - 2) else 0)
                exp_part(u % 2, u, k_neg, k_exp, 4 * c + u + 1)

            def k_hi_tile(c, u):
                act.wait_ge(k_elu, 4 * c + u + 1)
                wait_past(act, g_done, 4 * c + u - 1)
                act.activation(feat16[:, u % 2, HI, :], feat[:, u % 2, :], ACT.Copy).then_inc(k_hi, 1)

            def copy_g(b):
                act.wait_ge(g_done, 4 * BATCH_CHUNKS * (b + 1))
                for bank in range(4):
                    act.activation(gT[:, b, bank // 2, bank % 2 * HALF:(bank % 2 + 1) * HALF], acc[:, bank, :],
                                   ACT.Copy).then_inc(g_copied, 1)

            def xn_hi_a(c, u):
                wait_past(act, g_done, 4 * c + u - 3)
                xn_hi(ln1, c, u)

            def a_chunk(c, b):
                for u in range(4):
                    if b and u == 0:
                        copy_g(b - 1)
                    k_exp_tile(c, u)
                    if live(*at(c, u + 2)):
                        xn_hi_a(*at(c, u + 2))
                    k_hi_tile(c, u)
                    if live(*at(c, u + 4)):
                        seed_rstd(ln1, *at(c, u + 4))

            act.wait_ge(consts_ready, 3)
            for u in range(4):
                seed_rstd(ln1, 0, u)
                if u >= 2:
                    xn_hi_a(0, u - 2)
            quads(act, a_chunk)
            copy_g(B - 1)

            def m_hi_jobs(part):
                first = sum(len(p) for p in CHAIN[:part])
                for n, (kind, b, i) in enumerate(CHAIN[part], first):
                    if kind == "m":
                        act.wait_ge(chain_full, n + 1)
                        act.wait_ge(rks_ready, b + 1)
                        for j in (2 * i, 2 * i + 1):
                            act.activation(m_at(b * BATCH_CHUNKS, HI, j), acc[:, n % 4, (j % 2) * D:(j % 2 + 1) * D],
                                           ACT.Copy, scale=rks[:, b, j:j + 1]).then_inc(m_hi, 1)

            def q_exp_tile(c, u):
                act.wait_ge(q_proj, 4 * c + u + 1)
                wait_past(act, q_lo, 4 * c + u - 1)
                exp_part(u % 2, u, q_neg, q_exp, 4 * c + u + 1)

            def q_hi_tile(c, u):
                act.wait_ge(q_norm, 4 * c + u + 1)
                if live(*at(c, u - 2)):
                    c2, u2 = at(c, u - 2)
                    act.wait_ge(qT_ready[u2], 16 * (c2 + 1))
                act.activation(feat16[:, u % 2, HI, :], feat[:, u % 2, :], ACT.Copy).then_inc(q_hi, 1)

            def xn_hi_b(c, u):
                wait_past(act, xn2T_ready[u], 16 * c)
                xn_hi(ln2, c, u)

            def relu_block(c, f):
                act.wait_ge(f1_done, FB * c + f + 1)
                wait_past(act, h_sq, FB * c + f - 1)
                act.activation(h_r[:, f % 2, :], acc[:, 2 + f % 2, :], ACT.Relu,
                               scale=1.0 / FC_SCALE ** 2).then_inc(h_relu, 1)

            def h_hi_block(c, par, f):
                act.wait_ge(h_sq, FB * c + f + 1)
                wait_past(act, f2_done, 4 * (c - 1))
                act.activation(h[:, par, HI, f, :], h_f[:, f % 4, :], ACT.Copy).then_inc(h_hi, 1)

            def b_chunk(s, par):
                for t in range(4):
                    if isinstance(s, int) and s == 0 and t >= 2:
                        m_hi_jobs(t)
                    if live(s, t):
                        q_exp_tile(s, t)
                    if live(*at(s, t - 4)):
                        xn_hi_b(*at(s, t - 4))
                    if live(s - 2):
                        relu_block(s - 2, 2 * t)
                        relu_block(s - 2, 2 * t + 1)
                    if live(s, t):
                        q_hi_tile(s, t)
                    if live(s - 2):
                        h_hi_block(s - 2, par, 2 * t)
                        h_hi_block(s - 2, par, 2 * t + 1)
                    if live(*at(s, t - 3)):
                        seed_rstd(ln2, *at(s, t - 3))

            act.wait_ge(g_done, TILES)
            act.wait_ge(k_lo, TILES)
            act.wait_ge(k_added, TILES + 1)
            act.wait_ge(w_split, 16)
            chunks(act, b_chunk)

        @block.vector
        def _(dve):
            def ln_stats(ln, src, c, u):
                dve.bn_stats(bn6[:, u, :], src).then_inc(ln.bn, 1)
                wait_apart(dve, ln.bn, 4 * c + u + 1, (consts_ready, 3))
                dve.bn_aggr(mv[:, u, :], bn6[:, u, :]).then_inc(ln.stats, 1)

            def ln_norm(ln, src, c, u):
                n = 3 * (4 * c + u)
                r0, p, q, r1 = seed[:, u:u + 1], newt[:, u, 0:1], newt[:, u, 1:2], newt[:, u, 2:3]
                dve.wait_ge(ln.seed, 4 * c + u + 1)
                dve.tensor_scalar(p, mv[:, u, 1:2], LN_EPS, r0, ALU.add, ALU.mult).then_inc(ln.newton, 1)
                dve.wait_ge(ln.newton, n + 1)
                dve.tensor_scalar(q, p, r0, -0.5, ALU.mult, ALU.mult).then_inc(ln.newton, 1)
                dve.wait_ge(ln.newton, n + 2)
                dve.tensor_scalar(r1, q, 1.5, r0, ALU.add, ALU.mult).then_inc(ln.newton, 1)
                dve.wait_ge(ln.newton, n + 3)
                dve.tensor_scalar(xn[:, u % 2, :], src, mv[:, u, 0:1], r1, ALU.subtract, ALU.mult).then_inc(ln.norm, 1)

            def xn_lo(ln, c, u):
                dve.wait_ge(ln.hi, 4 * c + u + 1)
                dve.tensor_tensor(xnat[:, u, LO, :], xn[:, u % 2, :], xnat[:, u, HI, :], ALU.subtract).then_inc(ln.lo, 1)

            def elu_plus_one(slot, u):
                return dve.scalar_tensor_tensor(out=feat[:, u % 2, :], in0=proj[:, slot, :], scalar=QK_SCALE,
                                                in1=feat[:, u % 2, :], op0=ALU.add, op1=ALU.max)

            split = [0]

            def split_piece(hi, lo, src, scale):
                dve.tensor_scalar(hi, src, scale, None, ALU.mult).then_inc(w_hi, 1)
                split[0] += 1
                dve.wait_ge(w_hi, split[0])
                dve.scalar_tensor_tensor(out=lo, in0=src, scalar=scale, in1=hi, op0=ALU.mult,
                                         op1=ALU.subtract).then_inc(w_split, 1)

            flat_k = [wk[:, part, :, :].rearrange("p c n -> p (c n)") for part in (HI, LO)]
            flat_q = [wq[:, part, :, :].rearrange("p c n -> p (c n)") for part in (HI, LO)]
            SPLIT = [None,
                     ("fc", FC_SCALE, 1, [wnat[:, 0, part, :] for part in (HI, LO)]),
                     ("proj", PROJ_SCALE, 2, [wnat[:, 1, part, :] for part in (HI, LO)]),
                     ("q", QK_SCALE, 3, flat_q)]

            def stats_a(c, u):
                wait_apart(dve, xa_loaded[u], 16 * (c + 1), (consts_ready, 3))
                ln_stats(ln1, x_t[:, u, :], c, u)

            def norm_a(c, u):
                ln_norm(ln1, x_t[:, u, :], c, u)

            def a_chunk(c, b):
                for u in range(4):
                    dve.wait_ge(k_exp, 4 * c + u + 1)
                    elu_plus_one(u % 2, u).then_inc(k_elu, 1)
                    if live(*at(c, u + 3)):
                        norm_a(*at(c, u + 3))
                    if live(*at(c, u + 2)):
                        xn_lo(ln1, *at(c, u + 2))
                    if live(*at(c, u + 4)):
                        stats_a(*at(c, u + 4))
                    if b:
                        name, scale, place, parts = SPLIT[b]
                        piece = slice(u * HALF, (u + 1) * HALF)
                        if u == 0:
                            dve.wait_ge(w_loaded[name], 16)
                        split_piece(parts[HI][:, piece], parts[LO][:, piece], stage[:, place, piece], scale)
                    dve.wait_ge(k_hi, 4 * c + u + 1)
                    dve.tensor_tensor(feat16[:, u % 2, LO, :], feat[:, u % 2, :], feat16[:, u % 2, HI, :],
                                      ALU.subtract).then_inc(k_lo, 1)

            dve.memset(ln16[:, :], float(np.log(QK_SCALE))).then_inc(consts_ready, 1)
            dve.memset(eps[:, :], LN_EPS).then_inc(consts_ready, 1)
            dve.memset(ones[:, :], 1.0).then_inc(consts_ready, 1)
            dve.wait_ge(consts_ready, 3)
            for u in range(4):
                stats_a(0, u)
            norm_a(0, 0)
            norm_a(0, 1)
            xn_lo(ln1, 0, 0)
            xn_lo(ln1, 0, 1)
            dve.wait_ge(w_loaded["k"], 16)
            for i in range(4):
                piece = slice(i * HALF, (i + 1) * HALF)
                split_piece(flat_k[HI][:, piece], flat_k[LO][:, piece], stage[:, 0, piece], QK_SCALE)
            norm_a(0, 2)
            quads(dve, a_chunk)

            def chain_reads(part):
                first = sum(len(p) for p in CHAIN[:part])
                for n, (kind, b, i) in enumerate(CHAIN[part], first):
                    bank = acc[:, n % 4, :]
                    dve.wait_ge(chain_full, n + 1)
                    if kind == "ksum":
                        o = b * HD + i * HALF
                        dve.tensor_copy(ks_all[:, o:o + HALF], bank).then_inc(ks_copied, 1)
                        dve.wait_ge(ks_copied, 2 * b + i + 1)
                        dve.nop().then_inc(chain_free, 1)
                    elif kind == "ksum column":
                        dve.reciprocal(rk[:, :], bank[:, 0:PAIRS]).then_inc(rk_ready, 1)
                        dve.wait_ge(rk_ready, b + 1)
                        dve.tensor_scalar(rks[:, b, :], rk[:, :], M_SCALE, None, ALU.mult).then_inc(rks_ready, 1)
                        dve.wait_ge(rks_ready, b + 1)
                        dve.nop().then_inc(chain_free, 1)
                    elif kind == "kv":
                        if i == 0 and b >= 2:
                            last_m = max(k for k, j in enumerate(JOBS) if j[:2] == ("m", b - 2))
                            dve.wait_ge(chain_full, last_m + 1)
                        src = bank.rearrange("p (j n) -> p j n", j=4)
                        for head in range(2):
                            own = slice(head * DH, (head + 1) * DH)
                            cp = dve.tensor_copy(kvT[own, b % 2, 4 * i:4 * i + 4, own], src[own, :, own])
                            if head:
                                cp.then_inc(kvT_ready, 1)
                        dve.wait_ge(kvT_ready, 2 * b + i + 1)
                        dve.nop().then_inc(chain_free, 1)
                    else:
                        dve.wait_ge(m_hi, PAIRS * b + 2 * i + 2)
                        dve.wait_ge(rks_ready, b + 1)
                        for j in (2 * i, 2 * i + 1):
                            lo = dve.scalar_tensor_tensor(
                                out=m_at(b * BATCH_CHUNKS, LO, j), in0=bank[:, (j % 2) * D:(j % 2 + 1) * D],
                                scalar=rks[:, b, j:j + 1], in1=m_at(b * BATCH_CHUNKS, HI, j), op0=ALU.mult, op1=ALU.subtract)
                        lo.then_inc(chain_free, 1)

            def spike_step(c, u, k):
                n = 5 * (4 * c + u) + k
                y = acc[:, 1, 0:D]
                level = THRESHOLDS[k] * PROJ_SCALE
                if k == 0:
                    dve.wait_ge(f2_done, 4 * c + u + 1)
                    wait_past(dve, out_ready, 4 * c + u)
                    dve.tensor_scalar(spikes[:, :], y, level, None, ALU.is_gt).then_inc(spike_steps, 1)
                else:
                    dve.wait_ge(spike_steps, n)
                    dve.scalar_tensor_tensor(out=spikes[:, :], in0=y, scalar=level, in1=spikes[:, :],
                                             op0=ALU.is_gt, op1=ALU.add).then_inc(spike_steps, 1)

            def write_out(c, u):
                dve.wait_ge(spike_steps, 5 * (4 * c + u) + 5)
                wait_past(dve, out_stored[u], 16 * c)
                dve.scalar_tensor_tensor(out=out_t[:, u, :], in0=spikes[:, :], scalar=1.0 / len(THRESHOLDS),
                                         in1=x2_at(c, u), op0=ALU.mult, op1=ALU.add).then_inc(out_ready, 1)

            def q_steps(c, u):
                slot, n = u % 2, 4 * c + u
                heads = feat[:, slot, :].rearrange("p (h d) -> p h d", h=H)
                dve.wait_ge(q_exp, n + 1)
                elu_plus_one(slot, u).then_inc(q_elu, 1)
                yield
                dve.wait_ge(q_elu, n + 1)
                dve.tensor_tensor(feat[:, slot, :], feat[:, slot, :], ks_at(c), ALU.mult).then_inc(q_ks, 1)
                yield
                dve.wait_ge(q_ks, n + 1)
                dve.tensor_reduce(zsum[:, slot, :], heads, AX.X, ALU.add).then_inc(q_z, 1)
                yield
                dve.wait_ge(q_z, n + 1)
                dve.tensor_scalar(zeps[:, slot, :], zsum[:, slot, :], Z_EPS * QK_SCALE ** 2, 1.0 / QN_SCALE,
                                  ALU.add, ALU.mult).then_inc(q_zeps, 1)
                yield
                dve.wait_ge(q_zeps, n + 1)
                wait_past(dve, q_norm, n - 1)
                dve.reciprocal(rz[:, slot, :], zeps[:, slot, :]).then_inc(q_rz, 1)
                yield

            def residual(c, u):
                dve.wait_ge(o_done, 4 * c + u + 1)
                dve.wait_ge(x_biased, 4 * c + u + 1)
                dve.scalar_tensor_tensor(out=x2_at(c, u), in0=acc[:, 0, 0:D], scalar=1.0 / (QN_SCALE * M_SCALE),
                                         in1=x_t[:, u, :], op0=ALU.mult, op1=ALU.add).then_inc(x2_done, 1)
                wait_apart(dve, x2_done, 4 * c + u + 1, (consts_ready, 3))
                ln_stats(ln2, x2_at(c, u), c, u)

            def square_block(c, f):
                dve.wait_ge(h_relu, FB * c + f + 1)
                wait_past(dve, h_lo, FB * c + f - 3)
                dve.tensor_tensor(h_f[:, f % 4, :], acc[:, 2 + f % 2, :], h_r[:, f % 2, :], ALU.mult).then_inc(h_sq, 1)

            def b_chunk(s, par):
                for t in range(4):
                    if isinstance(s, int) and s == 0:
                        chain_reads(t)
                    if live(*at(s, t - 4)):
                        c, u = at(s, t - 4)
                        ln_norm(ln2, x2_at(c, u), c, u)
                    steps = q_steps(s, t) if live(s, t) else iter(())
                    for k in range(5):
                        next(steps, None)
                        if live(s - 3):
                            spike_step(s - 3, t, k)
                    if live(s - 3):
                        write_out(s - 3, t)
                    if live(*at(s, t - 4)):
                        xn_lo(ln2, *at(s, t - 4))
                    if live(*at(s, t - 3)):
                        residual(*at(s, t - 3))
                    if live(s - 2):
                        square_block(s - 2, 2 * t)
                        square_block(s - 2, 2 * t + 1)

            for i in range(4):
                dve.wait_ge(w_turned[i], 16)
            dve.wait_ge(kvT_zeroed, 1)
            chunks(dve, b_chunk)

        @block.gpsimd
        def _(pool):
            pool.memset(kacc, 0.0).then_inc(k_added, 1)
            pool.memset(h_f[:, :, :], 0.0).then_inc(kvT_zeroed, 1)
            for b in range(B):
                with pool.Fori(b * BATCH_CHUNKS, (b + 1) * BATCH_CHUNKS) as c:
                    for u in range(4):
                        pool.wait_ge(k_elu, 4 * c + u + 1)
                        pool.wait_ge(k_added, 4 * c + u + 1)
                        pool.tensor_tensor(kacc[:, b, :], kacc[:, b, :], feat[:, u % 2, :], ALU.add).then_inc(k_added, 1)

            def bias_x(c, u):
                pool.wait_ge(xb_loaded[u], 16 * (c + 1))
                pool.tensor_tensor(x_t[:, u, :], x_t[:, u, :], bo_all[:, :], ALU.add).then_inc(x_biased, 1)

            def normalise_q(c, u):
                heads = feat[:, u % 2, :].rearrange("p (h d) -> p h d", h=H)
                pool.wait_ge(q_rz, 4 * c + u + 1)
                pool.tensor_tensor(heads, heads, rz[:, u % 2, :].unsqueeze(2).to_broadcast([P, H, DH]),
                                   ALU.mult).then_inc(q_norm, 1)

            def q_lo_tile(c, u):
                pool.wait_ge(q_hi, 4 * c + u + 1)
                pool.tensor_tensor(feat16[:, u % 2, LO, :], feat[:, u % 2, :], feat16[:, u % 2, HI, :],
                                   ALU.subtract).then_inc(q_lo, 1)

            def h_lo_block(c, par, f):
                pool.wait_ge(h_hi, FB * c + f + 1)
                pool.tensor_tensor(h[:, par, LO, f, :], h_f[:, f % 4, :], h[:, par, HI, f, :],
                                   ALU.subtract).then_inc(h_lo, 1)

            def b_chunk(s, par):
                for t in range(4):
                    if live(*at(s, t - 2)):
                        bias_x(*at(s, t - 2))
                    if live(s, t):
                        normalise_q(s, t)
                        q_lo_tile(s, t)
                    if live(s - 2):
                        h_lo_block(s - 2, par, 2 * t)
                        h_lo_block(s - 2, par, 2 * t + 1)

            pool.wait_ge(w_loaded["bo"], 16)
            chunks(pool, b_chunk)


_INS = ['L0_attn_x', 'L0_attn_Wq', 'L0_attn_Wk', 'L0_attn_Wv', 'L0_attn_Wo', 'L0_attn_bo', 'L0_ffn_W_fc', 'L0_ffn_W_proj']


def kernel(**inputs):
    import numpy as _np
    import concourse.bacc as _bacc
    from concourse import mybir as _mybir
    from concourse.bass_utils import run_bass_kernel_spmd as _run

    nc = _bacc.Bacc("TRN2", target_bir_lowering=False, num_devices=1)
    arrays, args = {}, []
    for name in _INS:
        a = _np.ascontiguousarray(inputs[name])
        arrays[f"in_{name}_dram"] = a
        args.append(nc.dram_tensor(f"in_{name}_dram", a.shape, _mybir.dt.from_np(a.dtype), kind="ExternalInput").ap())
    shape = arrays["in_L0_attn_x_dram"].shape
    args.append(nc.dram_tensor("out_0_dram", shape, _mybir.dt.float32, kind="ExternalOutput").ap())
    build(nc, *args)
    r = _run(nc, [arrays], core_ids=[0])
    return r.results[0]["out_0_dram"]
```

```python
from contextlib import ExitStack

import concourse.bass as bass
import numpy as np
from concourse import mybir

ACT = mybir.ActivationFunctionType
ALU = mybir.AluOpType
AX = mybir.AxisListType
F32 = mybir.dt.float32
F16 = mybir.dt.float16

P = 128
HI, LO = 0, 1
PRODUCTS = ((HI, HI), (HI, LO), (LO, HI))

LN_EPS = 1e-5
EXP_LN_SET = 6
Z_EPS = 1e-6
QK_SCALE = 16.0
FC_SCALE = 16.0
PROJ_SCALE = 256.0
QN_SCALE = 256.0
M_SCALE = 64.0


def spike_thresholds(beta=0.9, threshold=1.0, steps=5):
    f = np.float32

    def count(y):
        mem, n = f(0), 0
        for _ in range(steps):
            reset = f(1) if mem - f(threshold) > 0 else f(0)
            mem = f(f(f(beta) * mem) + y) - reset * f(threshold)
            n += int(mem - f(threshold) > 0)
        return n

    found = []
    for k in range(1, steps + 1):
        below, above = int(f(0.0).view(np.uint32)), int(f(4.0).view(np.uint32))
        while above - below > 1:
            mid = (below + above) // 2
            if count(np.uint32(mid).view(f)) >= k:
                above = mid
            else:
                below = mid
        found.append(float(np.uint32(below).view(f)))
    return found


def at(chunk, u):
    return chunk + u // 4, u % 4


def wait_past(eng, sem, count):
    if isinstance(count, int) and count <= 0:
        return
    eng.wait_ge(sem, count)


def wait_apart(eng, sem, count, met):
    if not isinstance(count, int):
        count = eng.snap(eng.to_reg(count))
        eng.wait_ge(*met)
    wait_past(eng, sem, count)


def build(nc, x_in, Wq_in, Wk_in, Wv_in, Wo_in, bo_in, Wfc_in, Wproj_in, out):
    B, N, D = x_in.shape
    HD = Wq_in.shape[1]
    F = Wfc_in.shape[0]
    DH = 64
    H = HD // DH
    C2 = D // P
    PAIRS = HD // P
    FB = F // P
    TILES = B * N // P
    CHUNKS = TILES // 4
    BATCH_CHUNKS = CHUNKS // B
    HALF = 512
    assert (D, HD, F, N) == (256, 1024, 1024, 2048)
    THRESHOLDS = spike_thresholds()

    x_rows = x_in.rearrange("b n d -> (b n) d")
    out_rows = out.rearrange("b n d -> (b n) d")
    xT_spill = nc.dram_tensor("xT_spill", [TILES * P, 2 * D], F16).ap()

    ctx = ExitStack()
    with ctx:
        def sb(name, shape, dt):
            return ctx.enter_context(nc.sbuf_tensor(name, shape, dt))

        def sem(name):
            return ctx.enter_context(nc.semaphore(name))

        def sems(name, n):
            return [sem(f"{name}{i}") for i in range(n)]

        wq = sb("wq", [P, 2, C2, HD], F16)
        wfcT = sb("wfcT", [P, 2, FB * C2, P], F16)
        wpT = sb("wpT", [P, 2, C2 * FB, P], F16)
        m_all = sb("m_all", [P, B * 2 * PAIRS * D], F16)
        stage = m_all[:, :].bitcast(F32).rearrange("p (w n) -> p w n", w=4)
        ks_all = sb("ks_all", [P, B * HD], F32)
        wnat = ks_all[:, :].bitcast(F16).rearrange("p (w h n) -> p w h n", w=2, h=2)
        qT = sb("qT", [P, 4, 2 * PAIRS, P], F16)
        kacc = qT[:, :, :, :].rearrange("p a b c -> p (a b c)").bitcast(F32).rearrange("p (b n) -> p b n", b=B)
        h = sb("h", [P, 2, 2, FB, HALF], F16)
        gT = h[:, :, :, :, :].rearrange("p a b c d -> p (a b c d)").bitcast(F32).rearrange(
            "p (b c n) -> p b c n", b=B, c=C2)
        x2 = sb("x2", [P, 16 * D], F32)
        wo = x2[:, 8 * D:8 * D + PAIRS * D].rearrange("p (j n) -> p j n", j=PAIRS)
        wv = sb("wv", [P, C2, HD], F32)
        xn2T = sb("xn2T", [P, 2, 2 * C2, HALF], F16)
        wk = xn2T[:, :, :, :].rearrange("p a b c -> p (a b c)").rearrange("p (h c n) -> p h c n", h=2, c=C2)
        h_f = sb("h_f", [P, 4, HALF], F32)
        kvT = h_f[:, :, :].rearrange("p a b -> p (a b)").rearrange("p (r j n) -> p r j n", r=2, j=PAIRS)
        h_r = sb("h_r", [P, 2, HALF], F32)
        feat = sb("feat", [P, 2, HD], F32)
        feat16 = sb("feat16", [P, 2, 2, HD], F16)
        xnat = sb("xnat", [P, 4, 2, D], F16)
        xT = sb("xT", [P, 4, 2 * C2, P], F16)
        x_t = sb("x_t", [P, 4, D], F32)
        xn = sb("xn", [P, 2, D], F32)
        out_t = sb("out_t", [P, 4, D], F32)
        spikes = sb("spikes", [P, D], F32)
        bo_all = sb("bo_all", [P, D], F32)
        ones = sb("ones", [P, P], F32)
        ln16 = sb("ln16", [P, 1], F32)
        eps = sb("eps", [P, 1], F32)
        bn6 = sb("bn6", [P, 4, 6], F32)
        mv = sb("mv", [P, 4, 2], F32)
        logv = sb("logv", [P, 4], F32)
        seed = sb("seed", [P, 4], F32)
        newt = sb("newt", [P, 4, 3], F32)
        zsum = sb("zsum", [P, 2, H], F32)
        zeps = sb("zeps", [P, 2, H], F32)
        rz = sb("rz", [P, 2, H], F32)
        rk = sb("rk", [P, PAIRS], F32)
        rks = sb("rks", [P, B, PAIRS], F32)

        proj = ctx.enter_context(nc.psum_tensor("proj", [P, 2, HD], F32))
        acc = ctx.enter_context(nc.psum_tensor("acc", [P, 4, HALF], F32))

        consts_ready = sem("consts_ready")
        kvT_zeroed = sem("kvT_zeroed")
        w_loaded = {n: sem(f"w_loaded_{n}") for n in ("fc", "proj", "q", "v", "o", "bo")}
        wk_loaded = sems("wk_loaded", 4)
        w_hi = sem("w_hi")
        w_split = sem("w_split")
        w_turned = sems("w_turned", 4)
        xa_loaded = sems("xa_loaded", 4)
        xnT_ready = sems("xnT_ready", 4)
        xnT_spilled = sems("xnT_spilled", 4)
        k_proj, k_neg, k_exp, k_elu = sem("k_proj"), sem("k_neg"), sem("k_exp"), sem("k_elu")
        k_hi, k_lo = sem("k_hi"), sem("k_lo")
        k_added = sem("k_added")
        g_done = sem("g_done")
        g_copied = [sem("g_copied_act"), sem("g_copied_dve")]
        chain_full = sem("chain_full")
        chain_free = sem("chain_free")
        ks_copied = sem("ks_copied")
        rks_ready = sem("rks_ready")
        m_hi = sem("m_hi")
        xT_loaded = sems("xT_loaded", 4)
        xb_loaded = sems("xb_loaded", 4)
        q_proj, q_neg, q_exp, q_elu = sem("q_proj"), sem("q_neg"), sem("q_exp"), sem("q_elu")
        q_ks, q_z, q_zeps, q_rz = sem("q_ks"), sem("q_z"), sem("q_zeps"), sem("q_rz")
        q_norm, q_hi, q_lo = sem("q_norm"), sem("q_hi"), sem("q_lo")
        qT_ready = sems("qT_ready", 4)
        o_done, x_biased, x2_done = sem("o_done"), sem("x_biased"), sem("x2_done")
        xn2T_ready = sems("xn2T_ready", 4)
        f1_done, h_relu, h_sq, h_hi, h_lo = (sem(n) for n in ("f1_done", "h_relu", "h_sq", "h_hi", "h_lo"))
        f2_done = sem("f2_done")
        spike_steps = sem("spike_steps")
        out_ready = sem("out_ready")
        out_stored = sems("out_stored", 4)

        class LayerNorm:

            def __init__(self, name):
                self.bn, self.stats = sem(name + "_bn"), sem(name + "_stats")
                self.log, self.seed = sem(name + "_log"), sem(name + "_seed")
                self.newton = sem(name + "_newton")
                self.norm, self.hi, self.lo = sem(name + "_norm"), sem(name + "_hi"), sem(name + "_lo")

        ln1, ln2 = LayerNorm("ln1"), LayerNorm("ln2")

        block = ctx.enter_context(nc.Block())

        def live(c, u=0):
            return not isinstance(c, int) or 0 <= 4 * c + u < TILES

        def rows(c, u):
            return bass.ds((4 * c + u) * P, P)

        def x2_at(c, u):
            return x2[:, bass.ds((c % 4) * (4 * D) + u * D, D)]

        def m_at(c, part, j):
            return m_all[:, bass.ds((c // BATCH_CHUNKS) * (2 * PAIRS * D) + (part * PAIRS + j) * D, D)]

        def ks_at(c):
            return ks_all[:, bass.ds((c // BATCH_CHUNKS) * HD, HD)]

        def last_of_a(c, u):
            return isinstance(c, int) and (c, u) == (CHUNKS, 0)

        def first_of_b(c, u):
            return isinstance(c, int) and (c, u) == (0, 0)

        def drains(c):
            return isinstance(c, int) and c >= CHUNKS - 2

        def y_at(c, u):
            return acc[:, 1 - (u % 2 if drains(c) else 0), 0:D]

        def quads(eng, body):
            for b in range(B):
                first = b * BATCH_CHUNKS
                body(first, b)
                end = first + BATCH_CHUNKS - (b == B - 1)
                with eng.Fori(first + 1, end) as c:
                    body(c, None)
            body(CHUNKS - 1, None)
            body(CHUNKS, None)

        def chunks(eng, body):
            for s in range(4):
                body(s, s % 2)
            with eng.Fori(0, (CHUNKS - 4) // 2) as i:
                body(2 * i + 4, 0)
                body(2 * i + 5, 1)
            for s in range(CHUNKS, CHUNKS + 4):
                body(s, s % 2)

        def kv_jobs(b):
            return [("ksum column", b, 0)] + [("kv", b, i) for i in range(2)]

        def m_jobs(b):
            return [("m", b, i) for i in range(PAIRS // 2)]

        CHAIN = {1: [("ksum", b, i) for b in range(B) for i in range(2)]}
        KSUMS = len(CHAIN[1])
        for b in range(B):
            CHAIN[2 * b + 1] = CHAIN.get(2 * b + 1, []) + kv_jobs(b)
            CHAIN[2 * b + 2] = m_jobs(b)
        JOBS = [job for part in CHAIN.values() for job in part]

        def chain_part(s, t):
            part = CHAIN.get(4 * s + t, []) if isinstance(s, int) else []
            return [(JOBS.index(job), *job) for job in part]

        def in_two(jobs):
            before = 2 if jobs and jobs[0][1] == "m" else len(jobs)
            return jobs[:before], jobs[before:]

        def through(*job):
            return JOBS.index(job) + 1

        def chain_bank(n):
            return proj[:, 1, n % 2 * HALF:(n % 2 + 1) * HALF] if n < KSUMS else acc[:, 1 + n % 3, :]

        def flat(w, part):
            return w[:, part, :, :].rearrange("p c n -> p (c n)")

        SPLIT = [("k", QK_SCALE, 0, [flat(wk, part) for part in (HI, LO)]),
                 ("fc", FC_SCALE, 1, [wnat[:, 0, part, :] for part in (HI, LO)]),
                 ("proj", PROJ_SCALE, 2, [wnat[:, 1, part, :] for part in (HI, LO)]),
                 ("q", QK_SCALE, 3, [flat(wq, part) for part in (HI, LO)])]

        def split_of(b, i):
            _, scale, place, parts = SPLIT[b]
            piece = slice(i * HALF, (i + 1) * HALF)
            return 4 * b + i, stage[:, place, piece], parts[HI][:, piece], parts[LO][:, piece], scale

        @block.sync
        def _(sp):
            met = (xa_loaded[0], 16)

            def load_x(c, u, loaded):
                sp.dma_start(x_t[:, u, :], x_rows[rows(c, u), :]).then_inc(loaded[u], 16)

            def load_piece(w, i):
                blocks, half = slice(2 * i, 2 * i + 2), slice(i % 2 * HALF, (i % 2 + 1) * HALF)
                if w == "fc":
                    src = Wfc_in.rearrange("(f p) d -> p f d", p=P)[:, blocks, :]
                elif w == "o":
                    src = Wo_in.rearrange("(j p) d -> p j d", p=P)[:, blocks, :]
                else:
                    src = {"k": Wk_in, "q": Wq_in, "v": Wv_in, "proj": Wproj_in}[w][i // 2 * P:(i // 2 + 1) * P, half]
                if w == "v":
                    dst = wv[:, i // 2, half]
                elif w == "o":
                    dst = wo[:, blocks, :]
                else:
                    place = [name for name, *_ in SPLIT].index(w)
                    dst = stage[:, place, i * HALF:(i + 1) * HALF]
                    if w == "fc":
                        dst = dst.rearrange("p (f d) -> p f d", f=2)
                sp.dma_start(dst, src).then_inc(wk_loaded[i] if w == "k" else w_loaded[w], 16)

            def turn_xn(c, u):
                wait_apart(sp, ln1.lo, 4 * c + u + 1, met)
                wait_apart(sp, k_proj, 4 * c + u - 3, met)
                wait_apart(sp, xnT_spilled[u], 16 * c, met)
                sp.dma_start_transpose(xT[:, u, :, :], xnat[:, u, :, :].rearrange("p h d -> p (h d)")
                                       ).then_inc(xnT_ready[u], 16)

            def spill_xn(c, u):
                wait_apart(sp, xnT_ready[u], 16 * (c + 1), met)
                sp.dma_start(xT_spill[rows(c, u), :], xT[:, u, :, :].rearrange("p a b -> p (a b)")
                             ).then_inc(xnT_spilled[u], 16)

            def load_x_a(c, u):
                wait_apart(sp, ln1.norm, 4 * c + u - 3, met)
                load_x(c, u, xa_loaded)

            load_x(0, 0, xa_loaded)
            load_x(0, 1, xa_loaded)
            for i in range(4):
                load_piece("k", i)
            load_x(0, 2, xa_loaded)
            load_x(0, 3, xa_loaded)
            sp.wait_ge(*met)
            turn_xn(0, 0)
            for u in range(4, 6):
                load_x_a(*at(0, u))
            turn_xn(0, 1)
            spill_xn(0, 0)

            def turn_weight(w, part, dst):
                sp.wait_ge(w_split, 8 + 4 * w)
                sp.dma_start_transpose(dst[:, part, :, :], wnat[:, w, part, :]).then_inc(w_turned[2 * w + part], 16)

            def a_chunk(c, loads=(), turns=()):
                for u in range(4):
                    if live(*at(c, u + 2)):
                        turn_xn(*at(c, u + 2))
                    if live(*at(c, u + 6)):
                        load_x_a(*at(c, u + 6))
                    if live(*at(c, u + 1)):
                        spill_xn(*at(c, u + 1))
                    for w in loads:
                        load_piece(w, u)
                    if u < len(turns):
                        turn_weight(*turns[u])

            a_chunk(0)
            a_chunk(1, loads=("fc", "v"))
            with sp.Fori(2, 6) as c:
                a_chunk(c)
            a_chunk(6, loads=("proj", "o"), turns=[(0, part, wfcT) for part in (HI, LO)])
            with sp.Fori(7, 10) as c:
                a_chunk(c)
            a_chunk(10, loads=("q",), turns=[(1, part, wpT) for part in (HI, LO)])
            sp.dma_start(bo_all[:, :], bo_in.partition_broadcast(P)).then_inc(w_loaded["bo"], 16)
            with sp.Fori(11, 14) as c:
                a_chunk(c)
            a_chunk(14)
            a_chunk(15)

            def load_xT(c, u):
                wait_apart(sp, q_proj, 4 * c + u - 3, met)
                sp.dma_start(xT[:, u, :, :].rearrange("p a b -> p (a b)"), xT_spill[rows(c, u), :]
                             ).then_inc(xT_loaded[u], 16)

            def load_x_b(c, u):
                wait_apart(sp, x2_done, 4 * c + u - 3, met)
                load_x(c, u, xb_loaded)

            def turn_q(c, u):
                wait_apart(sp, q_lo, 4 * c + u + 1, met)
                wait_apart(sp, o_done, 4 * c + u - 3, met)
                sp.dma_start_transpose(qT[:, u, :, :], feat16[:, u % 2, :, :].rearrange("p h n -> p (h n)")
                                       ).then_inc(qT_ready[u], 16)

            def turn_xn2(c, u, par):
                wait_apart(sp, ln2.lo, 4 * c + u + 1, met)
                wait_apart(sp, f1_done, FB * (c - 1), met)
                sp.dma_start_transpose(xn2T[:, par, :, u * P:(u + 1) * P], xnat[:, u, :, :].rearrange("p h d -> p (h d)")
                                       ).then_inc(xn2T_ready[u], 16)

            def store_out(c, u):
                wait_apart(sp, out_ready, 4 * c + u + 1, met)
                sp.dma_start(out_rows[rows(c, u), :], out_t[:, u, :]).then_inc(out_stored[u], 16)

            for u in range(3):
                sp.wait_ge(xnT_spilled[u], 16 * CHUNKS)
                sp.wait_ge(k_proj, TILES - 3 + u)
                load_xT(0, u)
            sp.wait_ge(xnT_spilled[3], 16 * CHUNKS)
            sp.wait_ge(k_proj, TILES)
            sp.wait_ge(ln1.norm, TILES)

            def b_chunk(s, par):
                for t in range(4):
                    if live(*at(s, t - 5)):
                        c, u = at(s, t - 5)
                        turn_xn2(c, u, (par + (t - 5) // 4) % 2)
                    if live(*at(s, t + 3)):
                        load_xT(*at(s, t + 3))
                    if live(s, t):
                        load_x_b(s, t)
                    if live(*at(s, t - 15)):
                        store_out(*at(s, t - 15))
                    if live(*at(s, t - 2)):
                        if isinstance(s, int) and 4 * s + t - 2 == 0:
                            sp.wait_ge(chain_full, KSUMS)
                        turn_q(*at(s, t - 2))

            for s in range(4):
                b_chunk(s, s % 2)
            with sp.Fori(0, (CHUNKS - 6) // 2) as i:
                b_chunk(2 * i + 4, 0)
                b_chunk(2 * i + 5, 1)
            for s in range(CHUNKS - 2, CHUNKS + 4):
                b_chunk(s, s % 2)
            for u in range(4):
                sp.wait_ge(out_stored[u], 16 * CHUNKS)

        @block.tensor
        def _(pe):
            def project(slot, u, w):
                for half in range(2):
                    n = 0
                    for c2 in range(C2):
                        for left, right in PRODUCTS:
                            n += 1
                            mm = pe.matmul(proj[:, slot, half * HALF:(half + 1) * HALF], xT[:, u, left * C2 + c2, :],
                                           w[:, right, c2, half * HALF:(half + 1) * HALF],
                                           start=(n == 1), stop=(n == C2 * len(PRODUCTS)))
                return mm

            def q_tile(c, u):
                pe.wait_ge(xT_loaded[u], 16 * (c + 1))
                wait_past(pe, q_elu, 4 * c + u - 1)
                project(u % 2, u, wq).then_inc(q_proj, 1)

            def k_tile(c, u):
                pe.wait_ge(xnT_ready[u], 16 * (c + 1))
                wait_past(pe, k_elu, 4 * c + u - 1)
                project(u % 2, u, wk).then_inc(k_proj, 1)

            def g_tile(c, u, first):
                pe.wait_ge(k_lo, 4 * c + u + 1)
                for c2 in range(C2):
                    for half in range(2):
                        if first:
                            wait_past(pe, g_copied[c2], 2 * (c // BATCH_CHUNKS - 1) + half + 1)
                        for n, (left, right) in enumerate(PRODUCTS):
                            mm = pe.matmul(acc[:, c2 * 2 + half, :], xnat[:, u, left, c2 * P:(c2 + 1) * P],
                                           feat16[:, u % 2, right, half * HALF:(half + 1) * HALF],
                                           start=(first and n == 0), stop=True, skip_group_check=True)
                mm.then_inc(g_done, 1)

            def a_chunk(c, b):
                for u in range(4):
                    if live(*at(c, u + 1)):
                        k_tile(*at(c, u + 1))
                    if last_of_a(c, u):
                        pe.wait_ge(w_split, 16)
                        pe.wait_ge(k_elu, TILES - 1)
                        q_tile(0, 0)
                    if live(*at(c, u - 1)):
                        g_tile(*at(c, u - 1), b is not None and u == 1)

            pe.wait_ge(w_split, 4)
            k_tile(0, 0)
            quads(pe, a_chunk)

            def chain_job(n, kind, b, i):
                bank = chain_bank(n)
                if n < KSUMS:
                    wait_past(pe, ks_copied, n - 1)
                else:
                    wait_past(pe, chain_free, n - KSUMS - 2)
                if kind == "ksum":
                    mm = pe.matmul(bank, ones[:, :], kacc[:, b, i * HALF:(i + 1) * HALF], start=True, stop=True)
                elif kind == "ksum column":
                    pe.wait_ge(ks_copied, through("ksum", b, 1))
                    for j in range(PAIRS):
                        o = b * HD + j * P
                        mm = pe.transpose(bank[:, j:j + 1], ks_all[0:1, o:o + P], ones[0:1, 0:1])
                elif kind == "kv":
                    for j in range(4 * i, 4 * i + 4):
                        for c2 in range(C2):
                            mm = pe.matmul(bank[:, (j % 4) * P:(j % 4 + 1) * P], wv[:, c2, j * P:(j + 1) * P],
                                           gT[:, b, c2, j * P:(j + 1) * P], start=(c2 == 0), stop=(c2 == C2 - 1))
                else:
                    pe.wait_ge(chain_free, through("kv", b, 1) - KSUMS)
                    for j in (2 * i, 2 * i + 1):
                        mm = pe.matmul(bank[:, (j % 2) * D:(j % 2 + 1) * D], kvT[:, b % 2, j, :], wo[:, j, :],
                                       start=True, stop=True)
                mm.then_inc(chain_full, 1)

            def o_tile(c, u):
                pe.wait_ge(qT_ready[u], 16 * (c + 1))
                wait_past(pe, x2_done, 4 * c + u)
                n = 0
                for j in range(PAIRS):
                    for left, right in PRODUCTS:
                        n += 1
                        mm = pe.matmul(acc[:, 0, 0:D], qT[:, u, left * PAIRS + j, :], m_at(c, right, j),
                                       start=(n == 1), stop=(n == PAIRS * len(PRODUCTS)))
                mm.then_inc(o_done, 1)

            def f1_block(c, par, f):
                if f == 0:
                    for u in range(4):
                        pe.wait_ge(xn2T_ready[u], 16 * (c + 1))
                wait_past(pe, h_relu, FB * c + f - 1)
                n = 0
                for c2 in range(C2):
                    for left, right in PRODUCTS:
                        n += 1
                        mm = pe.matmul(acc[:, 2 + f % 2, :], wfcT[:, left, f * C2 + c2, :], xn2T[:, par, right * C2 + c2, :],
                                       start=(n == 1), stop=(n == C2 * len(PRODUCTS)))
                mm.then_inc(f1_done, 1)

            def f1_quarter(c, par, quarter):
                f1_block(c, par, 2 * quarter)
                f1_block(c, par, 2 * quarter + 1)

            def f2_tile(c, par, u):
                one_by_one = isinstance(c, int) and (c, u) == (CHUNKS - 1, 0)
                if u == 0:
                    pe.wait_ge(h_lo, FB * (c + 1) - (2 if one_by_one else 0))
                ahead = drains(c) and (c, u) != (CHUNKS - 2, 0)
                wait_past(pe, spike_steps, 5 * (4 * c + u - ahead))
                n = 0
                for f in range(FB):
                    if one_by_one and f >= FB - 2:
                        pe.wait_ge(h_lo, FB * c + f + 1)
                    for left, right in PRODUCTS:
                        n += 1
                        mm = pe.matmul(y_at(c, u), h[:, par, left, f, u * P:(u + 1) * P], wpT[:, right, f::FB, :],
                                       start=(n == 1), stop=(n == FB * len(PRODUCTS)))
                mm.then_inc(f2_done, 1)

            def b_chunk(s, par):
                for t in range(4):
                    early, late = in_two(chain_part(s, t))
                    kv_step = bool(early) and early[0][1] == "ksum column"
                    if live(s, t) and kv_step:
                        q_tile(s, t)
                    for job in early:
                        if job[0] == 0:
                            pe.wait_ge(k_added, TILES + 1)
                            pe.wait_ge(k_elu, TILES)
                            pe.wait_ge(consts_ready, 2)
                        if job[0] == KSUMS:
                            pe.wait_ge(g_copied[0], 2 * B + 2)
                            pe.wait_ge(w_loaded["v"], 64)
                            pe.wait_ge(w_loaded["o"], 64)
                        chain_job(*job)
                    if live(s, t) and not (kv_step or first_of_b(s, t)):
                        if first_of_b(s, t - 1):
                            pe.wait_ge(ks_copied, KSUMS)
                        q_tile(s, t)
                    c, quarter = at(s, t - 9)
                    first_of_f1 = first_of_b(c, quarter)
                    if live(c, quarter) and not first_of_f1:
                        f1_quarter(c, (par + (t - 9) // 4) % 2, quarter)
                    c, u = at(s, t - 3)
                    if live(c, u):
                        if first_of_b(c, u):
                            pe.wait_ge(chain_free, through("m", 0, PAIRS // 2 - 1) - KSUMS)
                            pe.wait_ge(m_hi, PAIRS)
                        o_tile(c, u)
                    if first_of_f1:
                        pe.wait_ge(chain_free, len(JOBS) - KSUMS)
                        pe.wait_ge(m_hi, B * PAIRS)
                        for i in range(4):
                            pe.wait_ge(w_turned[i], 16)
                        f1_quarter(0, 0, 0)
                    for job in late:
                        chain_job(*job)
                    c, u = at(s, t - 13)
                    if live(c, u):
                        if isinstance(c, int) and (c, u) == (CHUNKS - 2, 0):
                            pe.wait_ge(x2_done, TILES)
                        f2_tile(c, (par + (t - 13) // 4) % 2, u)

            chunks(pe, b_chunk)

        @block.scalar
        def _(act):
            def seed_rstd(ln, c, u):
                act.wait_ge(ln.stats, 4 * c + u + 1)
                act.activation(logv[:, u:u + 1], mv[:, u, 1:2], ACT.Ln, bias=eps[:, :]).then_inc(ln.log, 1)
                act.wait_ge(ln.log, 4 * c + u + 1)
                act.activation(seed[:, u:u + 1], logv[:, u:u + 1], ACT.Exp, scale=-0.5).then_inc(ln.seed, 1)

            def xn_hi(ln, c, u):
                act.wait_ge(ln.norm, 4 * c + u + 1)
                act.activation(xnat[:, u, HI, :], xn[:, u % 2, :], ACT.Copy).then_inc(ln.hi, 1)

            def exp_part(slot, u, neg, exp, count):
                act.activation(feat[:, u % 2, :], proj[:, slot, :], ACT.Relu, scale=-1.0 / QK_SCALE).then_inc(neg, 1)
                act.wait_ge(neg, count)
                act.activation(feat[:, u % 2, :], feat[:, u % 2, :], ACT.Exp, bias=ln16[:, :], scale=-1.0).then_inc(exp, 1)

            def k_exp_tile(c, u):
                act.wait_ge(k_proj, 4 * c + u + 1)
                wait_past(act, k_lo, 4 * c + u - 1)
                wait_past(act, k_added, 4 * c + u if live(c, u - 2) else 0)
                exp_part(u % 2, u, k_neg, k_exp, 4 * c + u + 1)

            def k_hi_tile(c, u):
                act.wait_ge(k_elu, 4 * c + u + 1)
                wait_past(act, g_done, 4 * c + u - 1)
                act.activation(feat16[:, u % 2, HI, :], feat[:, u % 2, :], ACT.Copy).then_inc(k_hi, 1)

            def copy_g(b, banks):
                act.wait_ge(g_done, 4 * BATCH_CHUNKS * (b + 1))
                for bank in banks:
                    act.activation(gT[:, b, bank // 2, bank % 2 * HALF:(bank % 2 + 1) * HALF], acc[:, bank, :],
                                   ACT.Copy).then_inc(g_copied[0], 1)

            def split_hi(b, i):
                n, src, hi, _, scale = split_of(b, i)
                if b == 0:
                    act.wait_ge(wk_loaded[i], 16)
                elif i == 0:
                    act.wait_ge(w_loaded[SPLIT[b][0]], 64)
                act.activation(hi, src, ACT.Copy, scale=scale).then_inc(w_hi, 1)

            def xn_hi_a(c, u):
                wait_past(act, g_done, 4 * c + u - 3)
                xn_hi(ln1, c, u)

            def a_chunk(c, b):
                for u in range(4):
                    if live(*at(c, u - 1)):
                        k_hi_tile(*at(c, u - 1))
                    if live(*at(c, u + 2)):
                        xn_hi_a(*at(c, u + 2))
                    if b and u == 1:
                        copy_g(b - 1, (0, 1))
                    if live(c, u):
                        k_exp_tile(c, u)
                    if live(*at(c, u + 3)):
                        seed_rstd(ln1, *at(c, u + 3))
                    if b:
                        split_hi(b, u)

            nc.scalar.add_instruction(mybir.InstLoadActFuncSet(
                act_func_set_id=EXP_LN_SET, name=nc.get_next_instruction_name(), engine=mybir.EngineType.Activation))
            act.wait_ge(consts_ready, 3)
            seed_rstd(ln1, 0, 0)
            xn_hi_a(0, 0)
            for i in range(4):
                split_hi(0, i)
            seed_rstd(ln1, 0, 1)
            xn_hi_a(0, 1)
            seed_rstd(ln1, 0, 2)
            quads(act, a_chunk)

            def chain_read(n, kind, b, i):
                if kind == "ksum":
                    act.wait_ge(chain_full, n + 1)
                    o = b * HD + i * HALF
                    act.activation(ks_all[:, o:o + HALF], chain_bank(n), ACT.Copy).then_inc(ks_copied, 1)
                    if n < 4:
                        copy_g(B - 1, (n,))
                if kind == "m":
                    act.wait_ge(chain_full, n + 1)
                    act.wait_ge(rks_ready, b + 1)
                    for j in (2 * i, 2 * i + 1):
                        act.activation(m_at(b * BATCH_CHUNKS, HI, j), chain_bank(n)[:, (j % 2) * D:(j % 2 + 1) * D],
                                       ACT.Copy, scale=rks[:, b, j:j + 1]).then_inc(m_hi, 1)

            def q_exp_tile(c, u):
                act.wait_ge(q_proj, 4 * c + u + 1)
                wait_past(act, q_lo, 4 * c + u - 1)
                exp_part(u % 2, u, q_neg, q_exp, 4 * c + u + 1)

            def q_hi_tile(c, u):
                act.wait_ge(q_norm, 4 * c + u + 1)
                if live(*at(c, u - 2)):
                    c2, u2 = at(c, u - 2)
                    act.wait_ge(qT_ready[u2], 16 * (c2 + 1))
                act.activation(feat16[:, u % 2, HI, :], feat[:, u % 2, :], ACT.Copy).then_inc(q_hi, 1)

            def xn_hi_b(c, u):
                wait_past(act, xn2T_ready[u], 16 * c)
                xn_hi(ln2, c, u)

            def relu_block(c, f):
                act.wait_ge(f1_done, FB * c + f + 1)
                wait_past(act, h_sq, FB * c + f - 1)
                act.activation(h_r[:, f % 2, :], acc[:, 2 + f % 2, :], ACT.Relu,
                               scale=1.0 / FC_SCALE ** 2).then_inc(h_relu, 1)

            def square_block(c, f):
                act.wait_ge(h_relu, FB * c + f + 1)
                wait_past(act, h_lo, FB * c + f - 3)
                act.activation(h_f[:, f % 4, :], h_r[:, f % 2, :], ACT.Square, scale=FC_SCALE).then_inc(h_sq, 1)

            def h_hi_block(c, par, f):
                act.wait_ge(h_sq, FB * c + f + 1)
                wait_past(act, f2_done, 4 * (c - 1))
                act.activation(h[:, par, HI, f, :], h_f[:, f % 4, :], ACT.Copy).then_inc(h_hi, 1)

            def b_chunk(s, par):
                for t in range(4):
                    if live(*at(s, t - 4)):
                        seed_rstd(ln2, *at(s, t - 4))
                    c, quarter = at(s, t - 9)
                    blocks = (2 * quarter, 2 * quarter + 1) if live(c, quarter) else ()
                    for f in blocks:
                        relu_block(c, f)
                    for f in blocks:
                        square_block(c, f)
                    early, late = in_two(chain_part(s, t))
                    for job in early:
                        chain_read(*job)
                    if live(s, t) and not first_of_b(s, t):
                        q_exp_tile(s, t)
                    for job in late:
                        chain_read(*job)
                    if live(*at(s, t - 4)):
                        xn_hi_b(*at(s, t - 4))
                    for f in blocks:
                        h_hi_block(c, (par + (t - 9) // 4) % 2, f)
                    if live(*at(s, t - 1)):
                        q_hi_tile(*at(s, t - 1))

            act.wait_ge(k_lo, TILES - 1)
            act.wait_ge(k_added, TILES)
            q_exp_tile(0, 0)
            for i in range(4):
                act.wait_ge(w_turned[i], 16)
            act.wait_ge(k_lo, TILES)
            act.wait_ge(k_added, TILES + 1)
            act.wait_ge(w_split, 16)
            chunks(act, b_chunk)

        @block.vector
        def _(dve):
            def ln_stats(ln, src, c, u):
                dve.bn_stats(bn6[:, u, :], src).then_inc(ln.bn, 1)
                wait_apart(dve, ln.bn, 4 * c + u + 1, (consts_ready, 3))
                dve.bn_aggr(mv[:, u, :], bn6[:, u, :]).then_inc(ln.stats, 1)

            def ln_steps(ln, src, c, u):
                n = 3 * (4 * c + u)
                r0, p, q, r1 = seed[:, u:u + 1], newt[:, u, 0:1], newt[:, u, 1:2], newt[:, u, 2:3]
                dve.wait_ge(ln.seed, 4 * c + u + 1)
                dve.tensor_scalar(p, mv[:, u, 1:2], LN_EPS, r0, ALU.add, ALU.mult).then_inc(ln.newton, 1)
                yield
                dve.wait_ge(ln.newton, n + 1)
                dve.tensor_scalar(q, p, r0, -0.5, ALU.mult, ALU.mult).then_inc(ln.newton, 1)
                yield
                dve.wait_ge(ln.newton, n + 2)
                dve.tensor_scalar(r1, q, 1.5, r0, ALU.add, ALU.mult).then_inc(ln.newton, 1)
                yield
                dve.wait_ge(ln.newton, n + 3)
                dve.tensor_scalar(xn[:, u % 2, :], src, mv[:, u, 0:1], r1, ALU.subtract, ALU.mult).then_inc(ln.norm, 1)

            def xn_lo(ln, c, u):
                dve.wait_ge(ln.hi, 4 * c + u + 1)
                dve.tensor_tensor(xnat[:, u, LO, :], xn[:, u % 2, :], xnat[:, u, HI, :], ALU.subtract).then_inc(ln.lo, 1)

            def elu_plus_one(slot, u):
                return dve.scalar_tensor_tensor(out=feat[:, u % 2, :], in0=proj[:, slot, :], scalar=QK_SCALE,
                                                in1=feat[:, u % 2, :], op0=ALU.add, op1=ALU.max)

            def split_lo(b, i):
                n, src, hi, lo, scale = split_of(b, i)
                dve.wait_ge(w_hi, n + 1)
                dve.scalar_tensor_tensor(out=lo, in0=src, scalar=scale, in1=hi, op0=ALU.mult,
                                         op1=ALU.subtract).then_inc(w_split, 1)

            def copy_g(b):
                dve.wait_ge(g_done, 4 * BATCH_CHUNKS * (b + 1))
                for half in range(2):
                    dve.tensor_copy(gT[:, b, 1, half * HALF:(half + 1) * HALF], acc[:, 2 + half, :]).then_inc(g_copied[1], 1)

            def stats_a(c, u):
                wait_apart(dve, xa_loaded[u], 16 * (c + 1), (consts_ready, 3))
                ln_stats(ln1, x_t[:, u, :], c, u)

            def norm_a(c, u):
                return ln_steps(ln1, x_t[:, u, :], c, u)

            def k_lo_tile(c, u):
                dve.wait_ge(k_hi, 4 * c + u + 1)
                dve.tensor_tensor(feat16[:, u % 2, LO, :], feat[:, u % 2, :], feat16[:, u % 2, HI, :],
                                  ALU.subtract).then_inc(k_lo, 1)

            def a_chunk(c, b):
                for u in range(4):
                    if live(*at(c, u + 2)):
                        for _ in norm_a(*at(c, u + 2)):
                            pass
                    if live(*at(c, u + 3)):
                        stats_a(*at(c, u + 3))
                    if live(*at(c, u - 1)):
                        k_lo_tile(*at(c, u - 1))
                    if live(*at(c, u + 2)):
                        xn_lo(ln1, *at(c, u + 2))
                    if b and u == 1:
                        copy_g(b - 1)
                    if b and u:
                        split_lo(b, u - 1)
                    if live(c, u):
                        dve.wait_ge(k_exp, 4 * c + u + 1)
                        elu_plus_one(u % 2, u).then_inc(k_elu, 1)
                    if b and u == 3:
                        split_lo(b, 3)

            dve.memset(ln16[:, :], float(np.log(QK_SCALE))).then_inc(consts_ready, 1)
            dve.memset(eps[:, :], LN_EPS).then_inc(consts_ready, 1)
            dve.memset(ones[:, :], 1.0).then_inc(consts_ready, 1)
            dve.wait_ge(consts_ready, 3)
            for u in range(2):
                stats_a(0, u)
            for u in range(2):
                for _ in norm_a(0, u):
                    pass
                xn_lo(ln1, 0, u)
                if u == 0:
                    for i in range(4):
                        split_lo(0, i)
            stats_a(0, 2)
            quads(dve, a_chunk)

            def chain_read(n, kind, b, i):
                bank = chain_bank(n)
                dve.wait_ge(chain_full, n + 1)
                if kind == "ksum column":
                    dve.reciprocal(rk[:, :], bank[:, 0:PAIRS]).then_inc(chain_free, 1)
                    dve.wait_ge(chain_free, n - KSUMS + 1)
                    dve.tensor_scalar(rks[:, b, :], rk[:, :], M_SCALE, None, ALU.mult).then_inc(rks_ready, 1)
                elif kind == "kv":
                    if i == 0 and b >= 2:
                        dve.wait_ge(chain_full, through("m", b - 2, PAIRS // 2 - 1))
                    src = bank.rearrange("p (j n) -> p j n", j=4)
                    for head in range(2):
                        own = slice(head * DH, (head + 1) * DH)
                        copied = dve.tensor_copy(kvT[own, b % 2, 4 * i:4 * i + 4, own], src[own, :, own])
                    copied.then_inc(chain_free, 1)
                else:
                    dve.wait_ge(m_hi, PAIRS * b + 2 * i + 2)
                    dve.wait_ge(rks_ready, b + 1)
                    for j in (2 * i, 2 * i + 1):
                        lo = dve.scalar_tensor_tensor(
                            out=m_at(b * BATCH_CHUNKS, LO, j), in0=bank[:, (j % 2) * D:(j % 2 + 1) * D],
                            scalar=rks[:, b, j:j + 1], in1=m_at(b * BATCH_CHUNKS, HI, j), op0=ALU.mult, op1=ALU.subtract)
                    lo.then_inc(chain_free, 1)

            def spike_step(c, u, k):
                n = 5 * (4 * c + u) + k
                y = y_at(c, u)
                level = THRESHOLDS[k] * PROJ_SCALE
                if k == 0:
                    dve.wait_ge(f2_done, 4 * c + u + 1)
                    wait_past(dve, out_ready, 4 * c + u)
                    dve.tensor_scalar(spikes[:, :], y, level, None, ALU.is_gt).then_inc(spike_steps, 1)
                else:
                    dve.wait_ge(spike_steps, n)
                    dve.scalar_tensor_tensor(out=spikes[:, :], in0=y, scalar=level, in1=spikes[:, :],
                                             op0=ALU.is_gt, op1=ALU.add).then_inc(spike_steps, 1)

            def write_out(c, u):
                dve.wait_ge(spike_steps, 5 * (4 * c + u) + 5)
                wait_past(dve, out_stored[u], 16 * c)
                dve.scalar_tensor_tensor(out=out_t[:, u, :], in0=spikes[:, :], scalar=1.0 / len(THRESHOLDS),
                                         in1=x2_at(c, u), op0=ALU.mult, op1=ALU.add).then_inc(out_ready, 1)

            def q_elu_tile(c, u):
                dve.wait_ge(q_exp, 4 * c + u + 1)
                elu_plus_one(u % 2, u).then_inc(q_elu, 1)

            def q_steps(c, u):
                slot, n = u % 2, 4 * c + u
                heads = feat[:, slot, :].rearrange("p (h d) -> p h d", h=H)
                if not first_of_b(c, u):
                    q_elu_tile(c, u)
                yield
                dve.wait_ge(q_elu, n + 1)
                if isinstance(c, int) and n == 0:
                    dve.wait_ge(ks_copied, through("ksum", 0, 1))
                if isinstance(c, int) and n == 1:
                    dve.wait_ge(ks_copied, KSUMS)
                dve.tensor_tensor(feat[:, slot, :], feat[:, slot, :], ks_at(c), ALU.mult).then_inc(q_ks, 1)
                yield
                dve.wait_ge(q_ks, n + 1)
                dve.tensor_reduce(zsum[:, slot, :], heads, AX.X, ALU.add).then_inc(q_z, 1)
                yield
                dve.wait_ge(q_z, n + 1)
                dve.tensor_scalar(zeps[:, slot, :], zsum[:, slot, :], Z_EPS * QK_SCALE ** 2, 1.0 / QN_SCALE,
                                  ALU.add, ALU.mult).then_inc(q_zeps, 1)
                yield
                dve.wait_ge(q_zeps, n + 1)
                wait_past(dve, q_norm, n - 1)
                dve.reciprocal(rz[:, slot, :], zeps[:, slot, :]).then_inc(q_rz, 1)
                yield

            def residual(c, u):
                dve.wait_ge(o_done, 4 * c + u + 1)
                dve.wait_ge(x_biased, 4 * c + u + 1)
                dve.scalar_tensor_tensor(out=x2_at(c, u), in0=acc[:, 0, 0:D], scalar=1.0 / (QN_SCALE * M_SCALE),
                                         in1=x_t[:, u, :], op0=ALU.mult, op1=ALU.add).then_inc(x2_done, 1)

            def stats_b(c, u):
                wait_apart(dve, x2_done, 4 * c + u + 1, (consts_ready, 3))
                ln_stats(ln2, x2_at(c, u), c, u)

            def b_chunk(s, par):
                for t in range(4):
                    early, late = in_two([job for job in chain_part(s, t) if job[1] != "ksum"])
                    if first_of_b(s, t - 1):
                        early, late = [], early
                    q = q_steps(*at(s, t - 1)) if live(*at(s, t - 1)) else iter(())
                    for k in range(5):
                        next(q, None)
                        for job in early[2 * k:2 * k + 2]:
                            chain_read(*job)
                        if live(*at(s, t - 14)):
                            spike_step(*at(s, t - 14), k)
                    if live(*at(s, t - 14)):
                        write_out(*at(s, t - 14))
                    c, u = at(s, t - 4)
                    if live(c, u):
                        for _ in ln_steps(ln2, x2_at(c, u), c, u):
                            pass
                    if live(*at(s, t - 3)):
                        residual(*at(s, t - 3))
                    if live(*at(s, t - 4)):
                        xn_lo(ln2, *at(s, t - 4))
                    if live(*at(s, t - 3)):
                        stats_b(*at(s, t - 3))
                    for job in late:
                        chain_read(*job)

            dve.wait_ge(kvT_zeroed, 1)
            q_elu_tile(0, 0)
            chunks(dve, b_chunk)

        @block.gpsimd
        def _(pool):
            pool.memset(kacc, 0.0).then_inc(k_added, 1)
            pool.memset(h_f[:, :, :], 0.0).then_inc(kvT_zeroed, 1)
            for b in range(B):
                with pool.Fori(b * BATCH_CHUNKS, (b + 1) * BATCH_CHUNKS) as c:
                    for u in range(4):
                        pool.wait_ge(k_elu, 4 * c + u + 1)
                        pool.wait_ge(k_added, 4 * c + u + 1)
                        pool.tensor_tensor(kacc[:, b, :], kacc[:, b, :], feat[:, u % 2, :], ALU.add).then_inc(k_added, 1)

            def bias_x(c, u):
                pool.wait_ge(xb_loaded[u], 16 * (c + 1))
                pool.tensor_tensor(x_t[:, u, :], x_t[:, u, :], bo_all[:, :], ALU.add).then_inc(x_biased, 1)

            def normalise_q(c, u):
                heads = feat[:, u % 2, :].rearrange("p (h d) -> p h d", h=H)
                pool.wait_ge(q_rz, 4 * c + u + 1)
                pool.tensor_tensor(heads, heads, rz[:, u % 2, :].unsqueeze(2).to_broadcast([P, H, DH]),
                                   ALU.mult).then_inc(q_norm, 1)

            def q_lo_tile(c, u):
                pool.wait_ge(q_hi, 4 * c + u + 1)
                pool.tensor_tensor(feat16[:, u % 2, LO, :], feat[:, u % 2, :], feat16[:, u % 2, HI, :],
                                   ALU.subtract).then_inc(q_lo, 1)

            def h_lo_block(c, par, f):
                pool.wait_ge(h_hi, FB * c + f + 1)
                pool.tensor_tensor(h[:, par, LO, f, :], h_f[:, f % 4, :], h[:, par, HI, f, :],
                                   ALU.subtract).then_inc(h_lo, 1)

            def b_chunk(s, par):
                for t in range(4):
                    if live(*at(s, t - 2)):
                        q_lo_tile(*at(s, t - 2))
                        bias_x(*at(s, t - 2))
                    if live(*at(s, t - 1)):
                        normalise_q(*at(s, t - 1))
                    c, quarter = at(s, t - 9)
                    if live(c, quarter):
                        h_lo_block(c, (par + (t - 9) // 4) % 2, 2 * quarter)
                        h_lo_block(c, (par + (t - 9) // 4) % 2, 2 * quarter + 1)

            pool.wait_ge(w_loaded["bo"], 16)
            chunks(pool, b_chunk)


_INS = ['L0_attn_x', 'L0_attn_Wq', 'L0_attn_Wk', 'L0_attn_Wv', 'L0_attn_Wo', 'L0_attn_bo', 'L0_ffn_W_fc', 'L0_ffn_W_proj']


def kernel(**inputs):
    import numpy as _np
    import concourse.bacc as _bacc
    from concourse import mybir as _mybir
    from concourse.bass_utils import run_bass_kernel_spmd as _run

    nc = _bacc.Bacc("TRN2", target_bir_lowering=False, num_devices=1)
    arrays, args = {}, []
    for name in _INS:
        a = _np.ascontiguousarray(inputs[name])
        arrays[f"in_{name}_dram"] = a
        args.append(nc.dram_tensor(f"in_{name}_dram", a.shape, _mybir.dt.from_np(a.dtype), kind="ExternalInput").ap())
    shape = arrays["in_L0_attn_x_dram"].shape
    args.append(nc.dram_tensor("out_0_dram", shape, _mybir.dt.float32, kind="ExternalOutput").ap())
    build(nc, *args)
    r = _run(nc, [arrays], core_ids=[0])
    return r.results[0]["out_0_dram"]
```
